# Optimizing a Trainium2 kernel written in Bass

```python
import numpy as np
import jax
import jax.numpy as jnp

def _softmax(x, axis=-1):
    return jax.nn.softmax(x, axis=axis)

def _gelu(x):
    return jax.nn.gelu(x, approximate=True)

def _silu(x):
    return jax.nn.silu(x)

def _sigmoid(x):
    return jax.nn.sigmoid(x)

def _layernorm(x, axis=-1, eps=1e-05):
    m = jnp.mean(x, axis=axis, keepdims=True)
    v = jnp.var(x, axis=axis, keepdims=True)
    return (x - m) / jnp.sqrt(v + eps)

def _scatter_add(tgt, idx, src, axis=0):
    return tgt.at[idx].add(src)

def _segment_sum(src, seg, n):
    return jax.ops.segment_sum(src, seg, n)
kernel_name = 'mk_rec_standalone_d1_rec_r8_3f2cf4'

def setup_inputs(seed: int=0):
    np.random.seed(seed)
    _w = jnp.asarray

    def _rec_inputs():
        import jax
        import jax.numpy as jnp
        _rk = jax.random.key(seed)
        r_embeddings = 7.22013e-05 + 1.00017 * jax.random.normal(jax.random.fold_in(_rk, 1), (2048, 32, 16), jnp.float32)
        return r_embeddings
    r_embeddings = _rec_inputs()

    def _L0_rec_setup():
        import jax, jax.numpy as jnp
        import numpy as np
        B, M, D = (2048, 32, 16)
        LAYERS = [64, 64, 64]
        key = jax.random.key(seed)
        ks = jax.random.split(key, 4)
        inp = {'embeddings': jax.random.normal(ks[0], (B, M, D), dtype=jnp.float32)}
        hk_1 = M
        for i, hk in enumerate(LAYERS):
            scale = (2.0 / (M * hk_1 + hk)) ** 0.5
            inp[f'W{i}'] = jax.random.normal(ks[i + 1], (M, hk_1, hk), dtype=jnp.float32) * scale
            hk_1 = hk
        return inp
    _L0_rec_all = _L0_rec_setup()
    _L0_rec_in = {k: v for k, v in _L0_rec_all.items() if k in ('W0', 'W1', 'W2')}
    del _L0_rec_all
    return {'r_embeddings': r_embeddings, 'L0_rec_W0': _L0_rec_in['W0'], 'L0_rec_W1': _L0_rec_in['W1'], 'L0_rec_W2': _L0_rec_in['W2']}

def reference(r_embeddings, L0_rec_W0, L0_rec_W1, L0_rec_W2):
    import jax
    import jax.numpy as jnp

    def _L0_rec_ref(embeddings, W0, W1, W2):
        import jax, jax.numpy as jnp
        import numpy as np
        B, M, D = (2048, 32, 16)
        LAYERS = [64, 64, 64]
        x0 = embeddings
        xk = x0
        outs = []
        for W in (W0, W1, W2):
            xk = jax.nn.relu(jnp.einsum('bmd,bhd,mhk->bkd', x0, xk, W))
            outs.append(jnp.sum(xk, axis=2))
        return jnp.concatenate(outs, axis=1)
    y = _L0_rec_ref(r_embeddings, L0_rec_W0, L0_rec_W1, L0_rec_W2)
    return y

_drawn_inputs = setup_inputs


def setup_inputs(seed=0):
    import zlib

    import numpy as np

    out = dict(_drawn_inputs(seed))
    spreads = {}
    factors = {}
    for name, (base, spread) in spreads.items():
        noise = np.random.default_rng([zlib.crc32(name.encode()), seed]).standard_normal(out[name].shape)
        drawn = base * np.exp(spread * noise) if base else spread * noise
        out[name] = jnp.asarray(drawn.astype(out[name].dtype))
    for name, factor in factors.items():
        out[name] = (out[name] * factor).astype(out[name].dtype)
    return out
```

```python
from contextlib import ExitStack

import concourse.bass as bass
from concourse import mybir

B, M, D, K = 2048, 32, 16, 64
Q = 4
BLK = 512
PAIRW = 2 * BLK
NPAIR = B * D // PAIRW
BB = BLK // D
A = M // Q
A0 = 5
NPERIOD = NPAIR // 2
PER_TRIP = 3
TRIPS = (NPERIOD - 1) // PER_TRIP
NX = 3
NZV, NZP = 3, 4
CH = 2
POOL_CH = 3
VEC_CH = 5

STAGES = [(0, 0), (2, -1), (0, 1), (1, 0), (1, 1), (2, 0)]
VEC_START = [0, 3, 8, 11, 16, 21]
VEC_ALL = 26
VEC_CHUNKS = [(0, 0), (0, 2), (0, 4), (1, 6), (0, 6)]
VEC_CHUNKS0 = [(0, 0), (0, 2), (0, 4)]
PE_ORDER = [("v", 0), ("g", 0), ("v", 1), ("v", 2), ("g", 1), ("v", 3), ("v", 4), ("g", 2)]
PE_ORDER0 = [("v", 0), ("v", 1), ("v", 2)]


class When:

    def __init__(self, tc, u=None):
        self.tc, self.u = tc, u

    def n(self, per_period, const):
        v = per_period * self.tc + const
        return v if self.u is None else self.u * (per_period * PER_TRIP) + v

    def back(self, periods):
        return When(self.tc - periods, self.u)


def set_ord(t, k):
    return (3, k // 2) if k % 2 == 0 else (3, k // 2 - 1)


def user_before(w, k):
    return (k - 2, 0) if k >= 2 and not (w.tc == 0 and k == 3) else (k + 4, 1)


def big_ord(k):
    return {1: -1, 3: 0, 4: 1, 5: 2}[k]


def vec_ord(tc, k):
    if tc == NPERIOD:
        return -VEC_CH
    return VEC_START[k] - (0 if tc == 0 and k == 0 else 5)


def vec_made(w, k, chunks):
    return w.n(VEC_ALL, vec_ord(w.tc, k) + chunks)


def pool_made(w, k, chunks=POOL_CH):
    return w.n(4 * POOL_CH, POOL_CH * big_ord(k) + chunks)


def landed(w, times):
    return 32 * times if w.u is None else w.u * 64 + 32 * times


def chunks_of(k):
    return VEC_CHUNKS if STAGES[k][0] else VEC_CHUNKS0


def half0_chunks(k):
    return 1 + max(i for i, (s, _) in enumerate(chunks_of(k)) if s == 0)


def half1_chunks(k):
    return 1 + max(i for i, (s, _) in enumerate(chunks_of(k)) if s == 1)


def build(nc, xt, w0, w0t, w1, w2, out):
    f32 = mybir.dt.float32
    ALU = mybir.AluOpType
    ACT = mybir.ActivationFunctionType
    AX = mybir.AxisListType
    N = NPAIR * PAIRW

    ctx = ExitStack()
    with ctx:
        def sb(name, shape):
            return ctx.enter_context(nc.sbuf_tensor(name, shape, f32))

        def ps(name, shape):
            return ctx.enter_context(nc.psum_tensor(name, shape, f32))

        def sem(name):
            return ctx.enter_context(nc.semaphore(name))

        twice = nc.dram_tensor("x0_twice", (2 * M, N), f32).ap()

        x0rot = sb("x0rot", [128, NX, A, PAIRW])
        x0rep = sb("x0rep", [128, 2, PAIRW])
        zv = sb("zv", [128, NZV, CH, PAIRW])
        zp = sb("zp", [128, NZP, CH, PAIRW])
        act_sb = sb("act_sb", [128, 2, BLK])
        half1 = sb("half1", [128, 2, PAIRW])
        w0_sb = sb("w0_sb", [128, A0, K])
        w0t_sb = sb("w0t_sb", [128, A0, K])
        w_sb = {1: sb("w1_sb", [128, A, 2, K]), 2: sb("w2_sb", [128, A, 2, K])}
        sums = sb("sums", [128, 3, NPAIR * BB])
        ident = sb("ident", [128, 128])

        xk0 = [ps(f"xk0_{i}", [128, PAIRW]) for i in range(2)]
        xk1 = ps("xk1", [128, PAIRW])
        acc = [ps(f"acc{i}", [128, BLK]) for i in range(2)]

        ident0 = sem("ident0")
        ident_made = sem("ident_made")
        w0_zeroed = sem("w0_zeroed")
        w0_landed = sem("w0_landed")
        w12_landed = {1: sem("w1_landed"), 2: sem("w2_landed")}
        w0_summed = sem("w0_summed")
        twice_made = [sem(f"twice_made{i}") for i in range(4)]
        x_landed = [[sem(f"x_landed{s}_{g}") for g in range(A // CH)] for s in range(NX)]
        rep_landed = [sem(f"rep_landed{i}") for i in range(2)]
        xk0_ready = [sem(f"xk0_ready{i}") for i in range(2)]
        xk1_ready = sem("xk1_ready")
        gates_passed = sem("gates_passed")
        half1_ready = sem("half1_ready")
        zv_ready, zv_used = sem("zv_ready"), sem("zv_used")
        zp_ready, zp_used = sem("zp_ready"), sem("zp_used")
        act_ready = [sem(f"act_ready{i}") for i in range(2)]
        act_summed = [sem(f"act_summed{i}") for i in range(2)]
        out_turned, out_copied, out_stored = sem("out_turned"), sem("out_copied"), sem("out_stored")

        def turned(g):
            bank = [xk0[0], xk0[1], xk1][(g // 2) % 3]
            return bank[:, BLK * (g % 2):BLK * (g % 2) + 3 * 128]

        block = ctx.enter_context(nc.Block())

        @block.sync
        def _(sp):
            cuts = [0, 2] + [2 + 10 * i for i in (1, 2, 3)]

            def make_twice(i):
                lo, hi = cuts[i] * PAIRW, cuts[i + 1] * PAIRW
                src = xt[:, lo:hi].unsqueeze(0).to_broadcast([2, M, hi - lo])
                dst = twice[:, lo:hi].rearrange("(two m) n -> two m n", two=2)
                sp.dma_start(dst, src).then_inc(twice_made[i], 16)

            def load_pair(p, slot, parity):
                cols = bass.ds(p * PAIRW, PAIRW)
                src = twice[0:M, cols].unsqueeze(0).to_broadcast([Q, M, PAIRW])
                sp.dma_start(x0rep[:, parity, :], src).then_inc(rep_landed[parity], 16)
                for a in range(A):
                    rows = [twice[Q * a + q:Q * a + q + M, cols] for q in range(Q)]
                    src = bass.AP(tensor=rows[0].tensor, offset=rows[0].offset, ap=[[N, Q], [N, M], [1, PAIRW]])
                    sp.dma_start(x0rot[:, slot, a, :], src).then_inc(x_landed[slot][a // CH], 16)

            make_twice(0)
            sp.wait_ge(w0_zeroed, 2)
            sp.dma_start(w0_sb[:, 0:4, :], w0[:, 0:4, :]).then_inc(w0_landed, 16)
            sp.dma_start(w0_sb[0:32, 4, :], w0[0:32, 4, :]).then_inc(w0_landed, 16)
            sp.dma_start(w0t_sb[32:128, 0, :], w0t[32:128, 0, :]).then_inc(w0_landed, 16)
            sp.dma_start(w0t_sb[:, 1:4, :], w0t[:, 1:4, :]).then_inc(w0_landed, 16)
            sp.wait_ge(twice_made[0], 16)
            load_pair(0, 0, 0)
            load_pair(1, 1, 1)
            sp.dma_start(w_sb[1][:], w1).then_inc(w12_landed[1], 16)
            sp.dma_start(w_sb[2][:], w2).then_inc(w12_landed[2], 16)
            make_twice(1)
            sp.wait_ge(twice_made[1], 16)
            sp.wait_ge(xk0_ready[0], 1)
            load_pair(2, 2, 0)
            make_twice(2)
            make_twice(3)
            sp.wait_ge(twice_made[2], 16)

            def next_pair(p, u=None):
                k, t = (5, (p - 3) // 2) if (p - 3) % 2 == 0 else (1, (p - 2) // 2)
                copied = When((p - 2) // 2, u).n(3, (p - 2) % 2 + 1)
                read_vec, read_pool = vec_made(When(t, u), k, VEC_CH), pool_made(When(t, u), k)
                sp.wait_ge(xk0_ready[0], copied)
                sp.sem_inc(gates_passed, 1)
                sp.wait_ge(zv_ready, read_vec)
                sp.sem_inc(gates_passed, 1)
                sp.wait_ge(zp_ready, read_pool)
                sp.sem_inc(gates_passed, 1)
                sp.wait_ge(twice_made[3], 16)
                load_pair(p if u is None else u * 6 + p, p % NX, p % 2)

            next_pair(3)
            with sp.Fori(0, 4) as u:
                for i in range(6):
                    next_pair(4 + i, u)
            for p in range(28, NPAIR):
                next_pair(p)

        @block.gpsimd
        def _(pool):
            nc.gpsimd.memset(w0_sb[:, 4, :], 0.0).then_inc(w0_zeroed, 1)
            nc.gpsimd.memset(w0t_sb[:], 0.0).then_inc(w0_zeroed, 1)
            nc.gpsimd.memset(ident[:], 0.0).then_inc(ident0, 1)
            pool.wait_ge(ident0, 1)
            nc.gpsimd.affine_select(out=ident[:], in_=ident[:], compare_op=ALU.not_equal, fill=1.0, base=0,
                                    pattern=[[-1, 128]], channel_multiplier=1).then_inc(ident_made, 1)

            def stage(w, k):
                layer, dp = STAGES[k]
                pc = 2 * w.tc + dp
                slot, times = pc % NX, pc // NX + 1
                o = big_ord(k)
                pool.wait_ge(half1_ready, w.n(4, o + 1))
                for c in range(POOL_CH):
                    if layer == 1:
                        pool.wait_ge(x_landed[slot][c], landed(w, times))
                    z = POOL_CH * (4 * w.tc + o) + c
                    if z >= NZP:
                        pool.wait_ge(zp_used, w.n(12, POOL_CH * o + c + 1 - NZP))
                    zi = z % NZP
                    i = nc.gpsimd.tensor_tensor(
                        zp[:, zi], x0rot[:, slot, CH * c:CH * c + CH, :],
                        half1[:, o % 2, :].unsqueeze(1).to_broadcast([128, CH, PAIRW]), ALU.mult)
                    i.then_inc(zp_ready, 1)

            def period(w):
                for k in (1, 3, 4, 5):
                    if not (w.tc == 0 and k == 1):
                        stage(w, k)

            period(When(0))
            with pool.Fori(0, TRIPS) as u:
                for j in range(PER_TRIP):
                    period(When(1 + j, u))
            stage(When(NPERIOD), 1)

        @block.vector
        def _(dve):
            dve.wait_ge(w0_landed, 64)
            nc.vector.tensor_tensor(w0_sb[:], w0_sb[:], w0t_sb[:], ALU.add).then_inc(w0_summed, 1)

            def sum_over_d(w, k):
                layer, dp = STAGES[k]
                per, c = set_ord(w, k)
                dve.wait_ge(act_ready[k % 2], w.n(per, c + 1))
                col = w.n(2 * BB, dp * BB)
                nc.vector.tensor_reduce(sums[:, layer, bass.ds(col, BB)],
                                        act_sb[:, k % 2, :].rearrange("p (b d) -> p b d", d=D),
                                        axis=AX.X, op=ALU.add).then_inc(act_summed[k % 2], 1)

            def stage(w, k):
                layer, dp = STAGES[k]
                pc = 2 * w.tc + dp
                slot, times = pc % NX, pc // NX + 1
                per, c0 = set_ord(w, k)
                zo = vec_ord(w.tc, k)
                chunks = VEC_CHUNKS if layer else VEC_CHUNKS0
                for c, (s, a) in enumerate(chunks):
                    if c == 0:
                        dve.wait_ge(xk0_ready[k % 2], w.n(per, c0 + 1))
                    if s == 1:
                        dve.wait_ge(xk1_ready, w.n(4, big_ord(k) + 1))
                    if layer < 2:
                        dve.wait_ge(x_landed[slot][a // CH], landed(w, times))
                    z = VEC_ALL * w.tc + zo + c
                    if z >= NZV:
                        dve.wait_ge(zv_used, w.n(VEC_ALL, zo + c + 1 - NZV))
                    na = CH if layer else min(CH, A0 - a)
                    xk = xk1 if s else xk0[k % 2]
                    i = nc.vector.tensor_tensor(
                        zv[:, z % NZV, 0:na], x0rot[:, slot, a:a + na, :],
                        xk[:, :].unsqueeze(1).to_broadcast([128, na, PAIRW]), ALU.mult)
                    i.then_inc(zv_ready, 1)
                    if c == 0:
                        if k >= 2 and not (w.tc == 0 and k == 3):
                            sum_over_d(w, k - 2)
                        elif k < 2 and w.tc > 0 and not (w.tc == NPERIOD):
                            sum_over_d(When(w.tc - 1, w.u), k + 4)

            def period(w):
                for k in range(6):
                    if not (w.tc == 0 and k == 1):
                        stage(w, k)

            period(When(0))
            with dve.Fori(0, TRIPS) as u:
                for j in range(PER_TRIP):
                    period(When(1 + j, u))
            sum_over_d(When(NPERIOD - 1), 4)
            stage(When(NPERIOD), 1)
            sum_over_d(When(NPERIOD - 1), 5)
            sum_over_d(When(NPERIOD), 1)

        @block.scalar
        def _(act):
            def relu(w, k):
                layer = STAGES[k][0]
                per, c = set_ord(w, k)
                if layer:
                    act.wait_ge(zp_used, pool_made(w, k))
                else:
                    act.wait_ge(zv_used, vec_made(w, k, len(VEC_CHUNKS0)))
                if w.u is not None or 3 * w.tc + c > 0:
                    act.wait_ge(act_summed[k % 2], w.n(per, c))
                readers = {2: 3, 4: 4, 5: 5, 0: 1}
                if k in readers and (k or w.tc):
                    kr = readers[k]
                    rper, rc = set_ord(w, kr)
                    act.wait_ge(half1_ready, w.n(4, big_ord(kr) + 1))
                    act.wait_ge(xk0_ready[kr % 2], w.n(rper, rc + 1))
                nc.scalar.activation(act_sb[:, k % 2, :], acc[k % 2][:, :], ACT.Relu).then_inc(act_ready[k % 2], 1)

            def source(k):
                return {3: (0, 0), 4: (2, 0), 5: (3, 0), 1: (4, 1)}[k]

            def wait_source(w, k):
                ks, back = source(k)
                per, c = set_ord(w, ks)
                act.wait_ge(act_ready[ks % 2], w.n(per, c + 1 - per * back))
                return ks % 2

            def fill(dst, parity, half):
                for blk in range(2):
                    row = K * blk + 32 * half
                    for q in range(Q):
                        last = nc.scalar.copy(dst[32 * q:32 * q + 32, BLK * blk:BLK * blk + BLK],
                                              act_sb[row:row + 32, parity, :])
                return last

            def fill_half1(w, k):
                parity = wait_source(w, k)
                o = big_ord(k)
                if w.u is not None or 4 * w.tc + o >= 2:
                    kb, back = {1: (4, 1), 3: (5, 1), 4: (1, 0), 5: (3, 0)}[k]
                    act.wait_ge(zp_ready, pool_made(w.back(back), kb))
                    act.wait_ge(xk1_ready, w.n(4, o - 1))
                fill(half1[:, o % 2, :], parity, 1).then_inc(half1_ready, 1)

            def fill_xk0(w, k):
                parity = wait_source(w, k)
                per, c = set_ord(w, k)
                if w.u is not None or 3 * w.tc + c > 0:
                    kb, back = user_before(w, k)
                    act.wait_ge(zv_ready, vec_made(w.back(back), kb, half0_chunks(kb)))
                fill(xk0[k % 2], parity, 0).then_inc(xk0_ready[k % 2], 1)

            def fill_xk1(w, k):
                o = big_ord(k)
                act.wait_ge(half1_ready, w.n(4, o + 1))
                if w.u is not None or 4 * w.tc + o > 0:
                    kb, back = {1: (5, 1), 3: (1, 0) if w.tc else (None, 0), 4: (3, 0), 5: (4, 0)}[k]
                    act.wait_ge(zv_ready, vec_made(w.back(back), kb, half1_chunks(kb)))
                for blk in range(2):
                    last = nc.scalar.copy(xk1[:, BLK * blk:BLK * blk + BLK],
                                          half1[:, o % 2, BLK * blk:BLK * blk + BLK])
                last.then_inc(xk1_ready, 1)

            def fill_x0(w, k):
                e = STAGES[k][1]
                per, c = set_ord(w, k)
                act.wait_ge(rep_landed[e], w.n(16, 16))
                if w.u is not None or 3 * w.tc + c > 0:
                    kb, back = user_before(w, k)
                    act.wait_ge(zv_ready, vec_made(w.back(back), kb, half0_chunks(kb)))
                for blk in range(2):
                    last = nc.scalar.copy(xk0[k % 2][:, BLK * blk:BLK * blk + BLK],
                                          x0rep[:, e, BLK * blk:BLK * blk + BLK])
                last.then_inc(xk0_ready[k % 2], 1)

            def period(w):
                first = w.tc == 0
                before = When(w.tc - 1, w.u)
                if not first:
                    fill_half1(w, 1)
                fill_x0(w, 0)
                if not first:
                    fill_xk0(w, 1)
                    relu(before, 5)
                    fill_xk1(w, 1)
                relu(w, 0)
                fill_x0(w, 2)
                fill_half1(w, 3)
                fill_xk0(w, 3)
                fill_xk1(w, 3)
                if not first:
                    relu(w, 1)
                relu(w, 2)
                fill_half1(w, 4)
                fill_xk0(w, 4)
                fill_xk1(w, 4)
                relu(w, 3)
                fill_half1(w, 5)
                fill_xk0(w, 5)
                fill_xk1(w, 5)
                relu(w, 4)

            period(When(0))
            with act.Fori(0, TRIPS) as u:
                for j in range(PER_TRIP):
                    period(When(1 + j, u))
            end = When(NPERIOD)
            fill_half1(end, 1)
            fill_xk0(end, 1)
            relu(When(NPERIOD - 1), 5)
            fill_xk1(end, 1)
            relu(end, 1)

            rows = zv[:, :, :, :].rearrange("p z a n -> p (z a n)")[:, 0:8 * 2 * 3 * K].rearrange(
                "p (g blk l k) -> p g blk l k", g=8, blk=2, l=3)
            for g in range(8):
                act.wait_ge(out_turned, g + 1)
                src = turned(g).rearrange("p (l blk k) -> p blk l k", l=3, blk=2)
                nc.scalar.copy(rows[:, g, 0], src[:, 0]).then_inc(out_copied, 1)
                nc.scalar.copy(rows[:, g, 1], src[:, 1]).then_inc(out_copied, 1)
                act.wait_ge(out_copied, 2 * g + 2)
                dst = out.rearrange("(blk g p) c -> g p blk c", blk=2, p=128)
                act.dma_start(dst[g], rows[:, g].rearrange("p blk l k -> p blk (l k)")).then_inc(out_stored, 16)
            act.wait_ge(out_stored, 8 * 16)

        @block.tensor
        def _(pe):
            def stage(w, k):
                layer, dp = STAGES[k]
                per, c0 = set_ord(w, k)
                if w.u is not None or 3 * w.tc + c0 > 0:
                    pe.wait_ge(act_ready[k % 2], w.n(per, c0))
                order = PE_ORDER if layer else PE_ORDER0
                for pos, (who, c) in enumerate(order):
                    if who == "v":
                        zo = vec_ord(w.tc, k)
                        pe.wait_ge(zv_ready, w.n(VEC_ALL, zo + c + 1))
                        s, a0 = (VEC_CHUNKS if layer else VEC_CHUNKS0)[c]
                        z = zv[:, (VEC_ALL * w.tc + zo + c) % NZV]
                    else:
                        o = big_ord(k)
                        pe.wait_ge(zp_ready, w.n(12, POOL_CH * o + c + 1))
                        s, a0 = 1, CH * c
                        z = zp[:, (POOL_CH * (4 * w.tc + o) + c) % NZP]
                    na = CH if layer else min(CH, A0 - a0)
                    for i in range(na):
                        lhsT = w_sb[layer][:, a0 + i, s, :] if layer else w0_sb[:, a0 + i, :]
                        first, end = pos == 0 and i == 0, pos == len(order) - 1 and i == na - 1
                        for blk in range(2):
                            last = nc.tensor.matmul(acc[k % 2][K * blk:K * blk + K, :], lhsT,
                                                    z[:, i, BLK * blk:BLK * blk + BLK], start=first, stop=end)
                    last.then_inc(zv_used if who == "v" else zp_used, 1)

            def period(w):
                for k in range(6):
                    if not (w.tc == 0 and k == 1):
                        if w.tc == 0 and k == 3:
                            pe.wait_ge(w12_landed[1], 16)
                        if w.tc == 0 and k == 5:
                            pe.wait_ge(w12_landed[2], 16)
                        stage(w, k)

            pe.wait_ge(w0_summed, 1)
            period(When(0))
            with pe.Fori(0, TRIPS) as u:
                for j in range(PER_TRIP):
                    period(When(1 + j, u))
            stage(When(NPERIOD), 1)

            pe.wait_ge(ident_made, 1)
            pe.wait_ge(act_summed[0], 3 * NPERIOD)
            pe.wait_ge(act_summed[1], 3 * NPERIOD)
            for g in range(8):
                if g >= 6:
                    pe.wait_ge(out_copied, 2 * (g - 6) + 2)
                for layer in range(3):
                    last = nc.tensor.transpose(turned(g)[:, 128 * layer:128 * layer + 128],
                                               sums[:, layer, 128 * g:128 * g + 128], ident[:])
                last.then_inc(out_turned, 1)


def kernel(r_embeddings, L0_rec_W0, L0_rec_W1, L0_rec_W2):
    import numpy as np
    import concourse.bacc as bacc
    from concourse.bass_utils import run_bass_kernel_spmd as run

    x = np.asarray(r_embeddings).reshape(2, NPAIR, BB, M, D)
    xt = np.ascontiguousarray(x.transpose(3, 1, 0, 2, 4).reshape(M, NPAIR * PAIRW))
    q, r, a, s = np.ix_(range(Q), range(32), range(A), range(2))
    w1 = np.ascontiguousarray(np.asarray(L0_rec_W1)[(r + Q * a + q) % M, 32 * s + r].reshape(128, A, 2, K))
    w2 = np.ascontiguousarray(np.asarray(L0_rec_W2)[(r + Q * a + q) % M, 32 * s + r].reshape(128, A, 2, K))
    q, r, a = np.ix_(range(Q), range(32), range(A))
    m, h = (r + Q * a + q) % M, r + 0 * a + 0 * q
    w0 = np.ascontiguousarray(np.asarray(L0_rec_W0)[m, h].reshape(128, A, K))
    w0t = np.ascontiguousarray(np.asarray(L0_rec_W0)[h, m].reshape(128, A, K))

    nc = bacc.Bacc("TRN2", target_bir_lowering=False, num_devices=1)
    arrays = {"xt": xt, "w0": w0, "w0t": w0t, "w1": w1, "w2": w2}
    args = [nc.dram_tensor(n, v.shape, mybir.dt.from_np(v.dtype), kind="ExternalInput").ap() for n, v in arrays.items()]
    args.append(nc.dram_tensor("out", (B, 3 * K), mybir.dt.float32, kind="ExternalOutput").ap())
    build(nc, *args)
    return run(nc, [arrays], core_ids=[0]).results[0]["out"]
```

```python
from contextlib import ExitStack

import concourse.bass as bass
from concourse import mybir

B, M, D, K = 2048, 32, 16, 64
Q = 4
BLK = 512
PAIRW = 2 * BLK
NPAIR = B * D // PAIRW
BB = BLK // D
A = M // Q
A0 = 5
NPERIOD = NPAIR // 2
PER_TRIP = 3
TRIPS = (NPERIOD - 1) // PER_TRIP
NX = 3
NZV, NZP = 3, 4
CH = 2
LOADS = [(0, 1), (2, 3), (4,), (5,), (6, 7)]
POOL_CH = 3
VEC_CH = 5

STAGES = [(0, 0), (2, -1), (0, 1), (1, 0), (1, 1), (2, 0)]
VEC_START = [0, 3, 8, 11, 16, 21]
VEC_ALL = 26
VEC_CHUNKS = [(0, 0), (0, 2), (0, 4), (1, 6), (0, 6)]
VEC_CHUNKS0 = [(0, 0), (0, 2), (0, 4)]
PE_ORDER = [("v", 0), ("g", 0), ("v", 1), ("v", 2), ("g", 1), ("v", 3), ("v", 4), ("g", 2)]
GROUPS = B // (2 * 128)
EARLY = GROUPS - 1
PE_ORDER0 = [("v", 0), ("v", 1), ("v", 2)]


class When:

    def __init__(self, tc, u=None):
        self.tc, self.u = tc, u

    def n(self, per_period, const):
        v = per_period * self.tc + const
        return v if self.u is None else self.u * (per_period * PER_TRIP) + v

    def back(self, periods):
        return When(self.tc - periods, self.u)


def set_ord(k):
    return (3, k // 2) if k % 2 == 0 else (3, k // 2 - 1)


def user_before(w, k):
    return (k - 2, 0) if k >= 2 and not (w.tc == 0 and k == 3) else (k + 4, 1)


def big_ord(k):
    return {1: -1, 3: 0, 4: 1, 5: 2}[k]


def vec_ord(tc, k):
    if tc == NPERIOD:
        return -VEC_CH
    return VEC_START[k] - (0 if tc == 0 and k == 0 else 5)


def vec_made(w, k, chunks):
    return w.n(VEC_ALL, vec_ord(w.tc, k) + chunks)


def pool_made(w, k, chunks=POOL_CH):
    return w.n(4 * POOL_CH, POOL_CH * big_ord(k) + chunks)


def loads_of(w, rotations, times):
    for g, rots in enumerate(LOADS):
        if set(rots) & set(rotations):
            n = 16 * len(rots)
            yield g, n * times if w.u is None else w.u * (n * 6 // NX) + n * times


def chunks_of(k):
    return VEC_CHUNKS if STAGES[k][0] else VEC_CHUNKS0


def half0_chunks(k):
    return 1 + max(i for i, (s, _) in enumerate(chunks_of(k)) if s == 0)


def half1_chunks(k):
    return 1 + max(i for i, (s, _) in enumerate(chunks_of(k)) if s == 1)


def build(nc, xt, w0, w0t, w1, w2, out):
    f32 = mybir.dt.float32
    ALU = mybir.AluOpType
    ACT = mybir.ActivationFunctionType
    AX = mybir.AxisListType
    N = NPAIR * PAIRW

    ctx = ExitStack()
    with ctx:
        def sb(name, shape):
            return ctx.enter_context(nc.sbuf_tensor(name, shape, f32))

        def ps(name, shape):
            return ctx.enter_context(nc.psum_tensor(name, shape, f32))

        def sem(name):
            return ctx.enter_context(nc.semaphore(name))

        twice = nc.dram_tensor("x0_twice", (2 * M, N), f32).ap()

        x0rot = sb("x0rot", [128, NX, A, PAIRW])
        x0rep = sb("x0rep", [128, 2, PAIRW])
        zv = sb("zv", [128, NZV, CH, PAIRW])
        zp = sb("zp", [128, NZP, CH, PAIRW])
        act_sb = sb("act_sb", [128, 2, BLK])
        half1 = sb("half1", [128, 2, PAIRW])
        w0_sb = sb("w0_sb", [128, A0, K])
        w0t_sb = sb("w0t_sb", [128, A0, K])
        w_sb = {1: sb("w1_sb", [128, A, 2, K]), 2: sb("w2_sb", [128, A, 2, K])}
        sums = sb("sums", [128, 3, NPAIR * BB])
        ident = sb("ident", [128, 128])

        xk0 = [ps(f"xk0_{i}", [128, PAIRW]) for i in range(2)]
        xk1 = ps("xk1", [128, PAIRW])
        acc = [ps(f"acc{i}", [128, BLK]) for i in range(2)]

        ident0 = sem("ident0")
        ident_made = sem("ident_made")
        w0_zeroed = sem("w0_zeroed")
        w0_landed = sem("w0_landed")
        w12_landed = {1: sem("w1_landed"), 2: sem("w2_landed")}
        w0_summed = sem("w0_summed")
        twice_made = [sem(f"twice_made{i}") for i in range(5)]
        x_landed = [[sem(f"x_landed{s}_{g}") for g in range(len(LOADS))] for s in range(NX)]
        rep_landed = [sem(f"rep_landed{i}") for i in range(2)]
        xk0_ready = [sem(f"xk0_ready{i}") for i in range(2)]
        xk1_ready = sem("xk1_ready")
        gates_passed = sem("gates_passed")
        half1_ready = sem("half1_ready")
        zv_ready, zv_used = sem("zv_ready"), sem("zv_used")
        zp_ready, zp_used = sem("zp_ready"), sem("zp_used")
        act_ready = [sem(f"act_ready{i}") for i in range(2)]
        act_summed = [sem(f"act_summed{i}") for i in range(2)]
        out_turned, out_copied, out_stored = sem("out_turned"), sem("out_copied"), sem("out_stored")

        rows = ctx.enter_context(nc.sbuf_tensor("rows", [128, 2, GROUPS, 3 * K], f32))

        def turned(g):
            return xk0[0][:, BLK * (g % 2):BLK * (g % 2) + 3 * 128]

        block = ctx.enter_context(nc.Block())

        @block.sync
        def _(sp):
            cuts = [0, 1, 2, 12, 22, 32]

            def make_twice(i):
                lo, hi = cuts[i] * PAIRW, cuts[i + 1] * PAIRW
                src = xt[:, lo:hi].unsqueeze(0).to_broadcast([2, M, hi - lo])
                dst = twice[:, lo:hi].rearrange("(two m) n -> two m n", two=2)
                sp.dma_start(dst, src).then_inc(twice_made[i], 16)

            def load_rep(cols, parity):
                src = xt[:, cols].unsqueeze(0).to_broadcast([Q, M, PAIRW])
                sp.dma_start(x0rep[:, parity, :], src).then_inc(rep_landed[parity], 16)

            def load_pair(p, slot, parity, rep=True, rotations=range(A)):
                cols = bass.ds(p * PAIRW, PAIRW)
                if rep:
                    load_rep(cols, parity)
                for a in rotations:
                    window = twice[Q * a:Q * a + M, cols]
                    src = bass.AP(tensor=window.tensor, offset=window.offset, ap=[[N, Q], [N, M], [1, PAIRW]])
                    g = next(g for g, rots in enumerate(LOADS) if a in rots)
                    sp.dma_start(x0rot[:, slot, a, :], src).then_inc(x_landed[slot][g], 16)

            make_twice(0)
            load_rep(bass.ds(0, PAIRW), 0)
            sp.wait_ge(w0_zeroed, 2)
            sp.dma_start(w0_sb[:, 0:4, :], w0[:, 0:4, :]).then_inc(w0_landed, 16)
            sp.dma_start(w0_sb[0:32, 4, :], w0[0:32, 4, :]).then_inc(w0_landed, 16)
            sp.dma_start(w0t_sb[32:128, 0, :], w0t[32:128, 0, :]).then_inc(w0_landed, 16)
            sp.dma_start(w0t_sb[:, 1:4, :], w0t[:, 1:4, :]).then_inc(w0_landed, 16)
            sp.wait_ge(twice_made[0], 16)
            load_pair(0, 0, 0, rep=False, rotations=range(2))
            make_twice(1)
            load_pair(0, 0, 0, rep=False, rotations=range(2, A0))
            sp.wait_ge(twice_made[1], 16)
            load_pair(1, 1, 1, rotations=range(2))
            sp.dma_start(w_sb[1][:], w1).then_inc(w12_landed[1], 16)
            load_pair(1, 1, 1, rep=False, rotations=range(2, A0))
            load_pair(0, 0, 0, rep=False, rotations=range(A0, A))
            load_pair(1, 1, 1, rep=False, rotations=range(A0, A))
            sp.dma_start(w_sb[2][:], w2).then_inc(w12_landed[2], 16)
            make_twice(2)
            sp.wait_ge(twice_made[2], 16)
            sp.wait_ge(xk0_ready[0], 1)
            load_pair(2, 2, 0)
            make_twice(3)
            make_twice(4)
            sp.wait_ge(twice_made[3], 16)

            def next_pair(p, u=None):
                k, t = (5, (p - 3) // 2) if (p - 3) % 2 == 0 else (1, (p - 2) // 2)
                copied = When((p - 2) // 2, u).n(3, (p - 2) % 2 + 1)
                read_vec, read_pool = vec_made(When(t, u), k, VEC_CH), pool_made(When(t, u), k)
                sp.wait_ge(xk0_ready[0], copied)
                sp.sem_inc(gates_passed, 1)
                sp.wait_ge(zv_ready, read_vec)
                sp.sem_inc(gates_passed, 1)
                sp.wait_ge(zp_ready, read_pool)
                sp.sem_inc(gates_passed, 1)
                sp.wait_ge(twice_made[4], 16)
                load_pair(p if u is None else u * 6 + p, p % NX, p % 2)

            next_pair(3)
            with sp.Fori(0, 4) as u:
                for i in range(6):
                    next_pair(4 + i, u)
            for p in range(28, NPAIR):
                next_pair(p)

            dst = out.rearrange("(blk g p) c -> p blk g c", blk=2, p=128)
            for blk in range(2):
                sp.wait_ge(out_copied, 2 * EARLY)
                sp.dma_start(dst[:, blk, 0:EARLY], rows[:, blk, 0:EARLY]).then_inc(out_stored, 16)
            sp.wait_ge(out_copied, 2 * GROUPS)
            sp.dma_start(dst[:, :, EARLY], rows[:, :, EARLY]).then_inc(out_stored, 16)
            sp.wait_ge(out_stored, 3 * 16)

        @block.gpsimd
        def _(pool):
            nc.gpsimd.memset(w0_sb[:, 4, :], 0.0).then_inc(w0_zeroed, 1)
            nc.gpsimd.memset(w0t_sb[:], 0.0).then_inc(w0_zeroed, 1)
            nc.gpsimd.memset(ident[:], 0.0).then_inc(ident0, 1)
            pool.wait_ge(ident0, 1)
            nc.gpsimd.affine_select(out=ident[:], in_=ident[:], compare_op=ALU.not_equal, fill=1.0, base=0,
                                    pattern=[[-1, 128]], channel_multiplier=1).then_inc(ident_made, 1)

            def stage(w, k):
                layer, dp = STAGES[k]
                pc = 2 * w.tc + dp
                slot, times = pc % NX, pc // NX + 1
                o = big_ord(k)
                pool.wait_ge(half1_ready, w.n(4, o + 1))
                for c in range(POOL_CH):
                    if layer == 1:
                        for g, n in loads_of(w, (CH * c, CH * c + 1), times):
                            pool.wait_ge(x_landed[slot][g], n)
                    z = POOL_CH * (4 * w.tc + o) + c
                    if z >= NZP:
                        pool.wait_ge(zp_used, w.n(12, POOL_CH * o + c + 1 - NZP))
                    zi = z % NZP
                    i = nc.gpsimd.tensor_tensor(
                        zp[:, zi], x0rot[:, slot, CH * c:CH * c + CH, :],
                        half1[:, o % 2, :].unsqueeze(1).to_broadcast([128, CH, PAIRW]), ALU.mult)
                    i.then_inc(zp_ready, 1)

            def period(w):
                for k in (1, 3, 4, 5):
                    if not (w.tc == 0 and k == 1):
                        stage(w, k)

            period(When(0))
            with pool.Fori(0, TRIPS) as u:
                for j in range(PER_TRIP):
                    period(When(1 + j, u))
            stage(When(NPERIOD), 1)

        @block.vector
        def _(dve):
            dve.wait_ge(w0_landed, 64)
            nc.vector.tensor_tensor(w0_sb[:], w0_sb[:], w0t_sb[:], ALU.add).then_inc(w0_summed, 1)

            def sum_over_d(w, k):
                layer, dp = STAGES[k]
                per, c = set_ord(k)
                dve.wait_ge(act_ready[k % 2], w.n(per, c + 1))
                col = w.n(2 * BB, dp * BB)
                nc.vector.tensor_reduce(sums[:, layer, bass.ds(col, BB)],
                                        act_sb[:, k % 2, :].rearrange("p (b d) -> p b d", d=D),
                                        axis=AX.X, op=ALU.add).then_inc(act_summed[k % 2], 1)

            def stage(w, k):
                layer, dp = STAGES[k]
                pc = 2 * w.tc + dp
                slot, times = pc % NX, pc // NX + 1
                per, c0 = set_ord(k)
                zo = vec_ord(w.tc, k)
                chunks = VEC_CHUNKS if layer else VEC_CHUNKS0
                for c, (s, a) in enumerate(chunks):
                    na = CH if layer else min(CH, A0 - a)
                    if c == 0:
                        dve.wait_ge(xk0_ready[k % 2], w.n(per, c0 + 1))
                    if s == 1:
                        dve.wait_ge(xk1_ready, w.n(4, big_ord(k) + 1))
                    if layer < 2:
                        for g, n in loads_of(w, range(a, a + na), times):
                            dve.wait_ge(x_landed[slot][g], n)
                    z = VEC_ALL * w.tc + zo + c
                    if z >= NZV:
                        dve.wait_ge(zv_used, w.n(VEC_ALL, zo + c + 1 - NZV))
                    xk = xk1 if s else xk0[k % 2]
                    i = nc.vector.tensor_tensor(
                        zv[:, z % NZV, 0:na], x0rot[:, slot, a:a + na, :],
                        xk[:, :].unsqueeze(1).to_broadcast([128, na, PAIRW]), ALU.mult)
                    i.then_inc(zv_ready, 1)
                    if c == 0:
                        if k >= 2 and not (w.tc == 0 and k == 3):
                            sum_over_d(w, k - 2)
                        elif k < 2 and w.tc > 0 and not (w.tc == NPERIOD):
                            sum_over_d(When(w.tc - 1, w.u), k + 4)

            def period(w):
                for k in range(6):
                    if not (w.tc == 0 and k == 1):
                        stage(w, k)

            period(When(0))
            with dve.Fori(0, TRIPS) as u:
                for j in range(PER_TRIP):
                    period(When(1 + j, u))
            sum_over_d(When(NPERIOD - 1), 4)
            stage(When(NPERIOD), 1)
            sum_over_d(When(NPERIOD - 1), 5)
            sum_over_d(When(NPERIOD), 1)

        @block.scalar
        def _(act):
            def relu(w, k):
                layer = STAGES[k][0]
                per, c = set_ord(k)
                if layer:
                    act.wait_ge(zp_used, pool_made(w, k))
                else:
                    act.wait_ge(zv_used, vec_made(w, k, len(VEC_CHUNKS0)))
                if w.u is not None or 3 * w.tc + c > 0:
                    act.wait_ge(act_summed[k % 2], w.n(per, c))
                readers = {2: 3, 4: 4, 5: 5, 0: 1}
                if k in readers and (k or w.tc):
                    kr = readers[k]
                    rper, rc = set_ord(kr)
                    act.wait_ge(half1_ready, w.n(4, big_ord(kr) + 1))
                    act.wait_ge(xk0_ready[kr % 2], w.n(rper, rc + 1))
                nc.scalar.activation(act_sb[:, k % 2, :], acc[k % 2][:, :], ACT.Relu).then_inc(act_ready[k % 2], 1)

            def wait_source(w, k):
                ks, back = {3: (0, 0), 4: (2, 0), 5: (3, 0), 1: (4, 1)}[k]
                per, c = set_ord(ks)
                act.wait_ge(act_ready[ks % 2], w.n(per, c + 1 - per * back))
                return ks % 2

            def fill(dst, parity, half):
                for blk in range(2):
                    row = K * blk + 32 * half
                    for q in range(Q):
                        last = nc.scalar.copy(dst[32 * q:32 * q + 32, BLK * blk:BLK * blk + BLK],
                                              act_sb[row:row + 32, parity, :])
                return last

            def fill_half1(w, k):
                parity = wait_source(w, k)
                o = big_ord(k)
                if w.u is not None or 4 * w.tc + o >= 2:
                    kb, back = {1: (4, 1), 3: (5, 1), 4: (1, 0), 5: (3, 0)}[k]
                    act.wait_ge(zp_ready, pool_made(w.back(back), kb))
                    act.wait_ge(xk1_ready, w.n(4, o - 1))
                fill(half1[:, o % 2, :], parity, 1).then_inc(half1_ready, 1)

            def fill_xk0(w, k):
                parity = wait_source(w, k)
                per, c = set_ord(k)
                if w.u is not None or 3 * w.tc + c > 0:
                    kb, back = user_before(w, k)
                    act.wait_ge(zv_ready, vec_made(w.back(back), kb, half0_chunks(kb)))
                fill(xk0[k % 2], parity, 0).then_inc(xk0_ready[k % 2], 1)

            def fill_xk1(w, k):
                o = big_ord(k)
                act.wait_ge(half1_ready, w.n(4, o + 1))
                if w.u is not None or 4 * w.tc + o > 0:
                    kb, back = {1: (5, 1), 3: (1, 0), 4: (3, 0), 5: (4, 0)}[k]
                    act.wait_ge(zv_ready, vec_made(w.back(back), kb, half1_chunks(kb)))
                for blk in range(2):
                    last = nc.scalar.copy(xk1[:, BLK * blk:BLK * blk + BLK],
                                          half1[:, o % 2, BLK * blk:BLK * blk + BLK])
                last.then_inc(xk1_ready, 1)

            def fill_x0(w, k):
                e = STAGES[k][1]
                per, c = set_ord(k)
                act.wait_ge(rep_landed[e], w.n(16, 16))
                if w.u is not None or 3 * w.tc + c > 0:
                    kb, back = user_before(w, k)
                    act.wait_ge(zv_ready, vec_made(w.back(back), kb, half0_chunks(kb)))
                for blk in range(2):
                    last = nc.scalar.copy(xk0[k % 2][:, BLK * blk:BLK * blk + BLK],
                                          x0rep[:, e, BLK * blk:BLK * blk + BLK])
                last.then_inc(xk0_ready[k % 2], 1)

            def period(w):
                first = w.tc == 0
                before = When(w.tc - 1, w.u)
                if not first:
                    fill_half1(w, 1)
                fill_x0(w, 0)
                if not first:
                    fill_xk0(w, 1)
                    relu(before, 5)
                    fill_xk1(w, 1)
                if first:
                    fill_x0(w, 2)
                relu(w, 0)
                if not first:
                    fill_x0(w, 2)
                if first:
                    fill_xk0(w, 3)
                fill_half1(w, 3)
                if not first:
                    fill_xk0(w, 3)
                fill_xk1(w, 3)
                if not first:
                    relu(w, 1)
                relu(w, 2)
                fill_half1(w, 4)
                fill_xk0(w, 4)
                fill_xk1(w, 4)
                relu(w, 3)
                fill_half1(w, 5)
                fill_xk0(w, 5)
                fill_xk1(w, 5)
                relu(w, 4)

            period(When(0))
            with act.Fori(0, TRIPS) as u:
                for j in range(PER_TRIP):
                    period(When(1 + j, u))
            end = When(NPERIOD)
            fill_half1(end, 1)
            fill_xk0(end, 1)
            relu(When(NPERIOD - 1), 5)
            fill_xk1(end, 1)

            def copy_rows(g):
                act.wait_ge(out_turned, g + 1)
                src = turned(g).rearrange("p (l blk k) -> p blk l k", l=3, blk=2)
                for blk in range(2):
                    nc.scalar.copy(rows[:, blk, g].rearrange("p (l k) -> p l k", l=3), src[:, blk]).then_inc(out_copied, 1)

            for g in range(EARLY):
                copy_rows(g)
            relu(end, 1)
            copy_rows(EARLY)

        @block.tensor
        def _(pe):
            def stage(w, k, between=None):
                layer, dp = STAGES[k]
                per, c0 = set_ord(k)
                if w.u is not None or 3 * w.tc + c0 > 0:
                    pe.wait_ge(act_ready[k % 2], w.n(per, c0))
                order = PE_ORDER if layer else PE_ORDER0
                for pos, (who, c) in enumerate(order):
                    if who == "v":
                        zo = vec_ord(w.tc, k)
                        pe.wait_ge(zv_ready, w.n(VEC_ALL, zo + c + 1))
                        s, a0 = (VEC_CHUNKS if layer else VEC_CHUNKS0)[c]
                        z = zv[:, (VEC_ALL * w.tc + zo + c) % NZV]
                    else:
                        o = big_ord(k)
                        pe.wait_ge(zp_ready, w.n(12, POOL_CH * o + c + 1))
                        s, a0 = 1, CH * c
                        z = zp[:, (POOL_CH * (4 * w.tc + o) + c) % NZP]
                    na = CH if layer else min(CH, A0 - a0)
                    for i in range(na):
                        lhsT = w_sb[layer][:, a0 + i, s, :] if layer else w0_sb[:, a0 + i, :]
                        first, end = pos == 0 and i == 0, pos == len(order) - 1 and i == na - 1
                        for blk in range(2):
                            last = nc.tensor.matmul(acc[k % 2][K * blk:K * blk + K, :], lhsT,
                                                    z[:, i, BLK * blk:BLK * blk + BLK], start=first, stop=end)
                    last.then_inc(zv_used if who == "v" else zp_used, 1)
                    if between:
                        between(pos)

            def period(w):
                for k in range(6):
                    if not (w.tc == 0 and k == 1):
                        if w.tc == 0 and k == 3:
                            pe.wait_ge(w12_landed[1], 16)
                        if w.tc == 0 and k == 5:
                            pe.wait_ge(w12_landed[2], 16)
                        stage(w, k)

            pe.wait_ge(w0_summed, 1)
            period(When(0))
            with pe.Fori(0, TRIPS) as u:
                for j in range(PER_TRIP):
                    period(When(1 + j, u))

            def turn(g):
                if g >= 2:
                    pe.wait_ge(out_copied, 2 * (g - 2) + 2)
                for layer in range(3):
                    last = nc.tensor.transpose(turned(g)[:, 128 * layer:128 * layer + 128],
                                               sums[:, layer, 128 * g:128 * g + 128], ident[:])
                last.then_inc(out_turned, 1)

            pe.wait_ge(ident_made, 1)
            for parity in range(2):
                pe.wait_ge(act_summed[parity], 3 * (NPERIOD - 2))
            pe.wait_ge(zv_ready, vec_made(When(NPERIOD - 1), 4, half0_chunks(4)))
            end = When(NPERIOD)
            stage(end, 1, between=lambda pos: [turn(g) for g in range(2 * pos, min(2 * pos + 2, EARLY))])
            pe.wait_ge(act_summed[0], 3 * NPERIOD)
            pe.wait_ge(act_summed[1], 3 * NPERIOD)
            turn(EARLY)


def kernel(r_embeddings, L0_rec_W0, L0_rec_W1, L0_rec_W2):
    import numpy as np
    import concourse.bacc as bacc
    from concourse.bass_utils import run_bass_kernel_spmd as run

    x = np.asarray(r_embeddings).reshape(2, NPAIR, BB, M, D)
    xt = np.ascontiguousarray(x.transpose(3, 1, 0, 2, 4).reshape(M, NPAIR * PAIRW))
    q, r, a, s = np.ix_(range(Q), range(32), range(A), range(2))
    w1 = np.ascontiguousarray(np.asarray(L0_rec_W1)[(r + Q * a + q) % M, 32 * s + r].reshape(128, A, 2, K))
    w2 = np.ascontiguousarray(np.asarray(L0_rec_W2)[(r + Q * a + q) % M, 32 * s + r].reshape(128, A, 2, K))
    q, r, a = np.ix_(range(Q), range(32), range(A))
    m, h = (r + Q * a + q) % M, r + 0 * a + 0 * q
    w0 = np.ascontiguousarray(np.asarray(L0_rec_W0)[m, h].reshape(128, A, K))
    w0t = np.ascontiguousarray(np.asarray(L0_rec_W0)[h, m].reshape(128, A, K))

    nc = bacc.Bacc("TRN2", target_bir_lowering=False, num_devices=1)
    arrays = {"xt": xt, "w0": w0, "w0t": w0t, "w1": w1, "w2": w2}
    args = [nc.dram_tensor(n, v.shape, mybir.dt.from_np(v.dtype), kind="ExternalInput").ap() for n, v in arrays.items()]
    args.append(nc.dram_tensor("out", (B, 3 * K), mybir.dt.float32, kind="ExternalOutput").ap())
    build(nc, *args)
    return run(nc, [arrays], core_ids=[0]).results[0]["out"]
```
